# Optimizing a Trainium2 kernel written in Bass

```python
import numpy as np
import jax
import jax.numpy as jnp

def _softmax(x, axis=-1):
    return jax.nn.softmax(x, axis=axis)

def _gelu(x):
    return jax.nn.gelu(x, approximate=True)

def _silu(x):
    return jax.nn.silu(x)

def _sigmoid(x):
    return jax.nn.sigmoid(x)

def _layernorm(x, axis=-1, eps=1e-05):
    m = jnp.mean(x, axis=axis, keepdims=True)
    v = jnp.var(x, axis=axis, keepdims=True)
    return (x - m) / jnp.sqrt(v + eps)

def _scatter_add(tgt, idx, src, axis=0):
    return tgt.at[idx].add(src)

def _segment_sum(src, seg, n):
    return jax.ops.segment_sum(src, seg, n)
kernel_name = 'mk_seq_preln_d1_jaxref_r4_8b9ab8'

def setup_inputs(seed: int=0):
    np.random.seed(seed)
    _w = jnp.asarray

    def _L0_attn_setup():
        import jax, jax.numpy as jnp
        import numpy as np
        B, T, D = (8, 1024, 512)
        K, V = (64, 128)

        def _gated_delta(x, Wq, Wk, Wv, Wo, Wb, bb, Wd, bd):
            q = jnp.einsum('btd,dk->btk', x, Wq)
            k = jnp.einsum('btd,dk->btk', x, Wk)
            v = jnp.einsum('btd,dv->btv', x, Wv)
            beta = jax.nn.sigmoid(jnp.einsum('btd,dk->btk', x, Wb) + bb)
            delta = jax.nn.softplus(jnp.einsum('btd,dk->btk', x, Wd) + bd)

            def step(S, inp):
                qt, kt, vt, bt, dt = inp
                kv = jnp.einsum('bk,bv->bkv', kt, vt)
                S = bt[:, :, None] * S + dt[:, :, None] * kv
                ot = jnp.einsum('bk,bkv->bv', qt, S)
                return (S, ot)
            S0 = jnp.zeros((x.shape[0], Wq.shape[1], Wv.shape[1]), dtype=x.dtype)
            xs = tuple((jnp.swapaxes(a, 0, 1) for a in (q, k, v, beta, delta)))
            _, outs = jax.lax.scan(step, S0, xs)
            out = jnp.swapaxes(outs, 0, 1)
            return jnp.einsum('btv,vd->btd', out, Wo)
        key = jax.random.key(seed)
        ks = jax.random.split(key, 9)
        s_d = 1.0 / np.sqrt(D)
        s_v = 1.0 / np.sqrt(V)
        return {'x': jax.random.normal(ks[0], (B, T, D), dtype=jnp.float32), 'Wq': jax.random.uniform(ks[1], (D, K), jnp.float32, -s_d, s_d), 'Wk': jax.random.uniform(ks[2], (D, K), jnp.float32, -s_d, s_d), 'Wv': jax.random.uniform(ks[3], (D, V), jnp.float32, -s_d, s_d), 'Wo': jax.random.uniform(ks[4], (V, D), jnp.float32, -s_v, s_v), 'Wb': jax.random.uniform(ks[5], (D, K), jnp.float32, -s_d, s_d), 'bb': jax.random.uniform(ks[6], (K,), jnp.float32, -s_d, s_d), 'Wd': jax.random.uniform(ks[7], (D, K), jnp.float32, -s_d, s_d), 'bd': jax.random.uniform(ks[8], (K,), jnp.float32, -s_d, s_d)}
    _L0_attn_in = _L0_attn_setup()

    def _L0_ffn_setup():
        import jax, jax.numpy as jnp
        import numpy as np
        EPS = 1e-08

        def _quantize(w):
            gamma = jnp.mean(jnp.abs(w))
            return jnp.clip(jnp.round(w / (gamma + EPS)), -1.0, 1.0)

        def _bitlinear(x, w):
            return jnp.matmul(x, _quantize(w).T)
        key = jax.random.key(seed)
        k1, k2, k3, k4 = jax.random.split(key, 4)
        d, h = (512, 1408)
        x = jax.random.normal(k1, (4, 512, d), dtype=jnp.float32)
        w1 = jax.random.normal(k2, (h, d), dtype=jnp.float32)
        w2 = jax.random.normal(k3, (h, d), dtype=jnp.float32)
        w3 = jax.random.normal(k4, (d, h), dtype=jnp.float32)
        return {'x': x, 'w1': w1, 'w2': w2, 'w3': w3}
    _L0_ffn_in = _L0_ffn_setup()
    _d = {'L0_attn_x': _L0_attn_in['x'], 'L0_attn_Wq': _L0_attn_in['Wq'], 'L0_attn_Wk': _L0_attn_in['Wk'], 'L0_attn_Wv': _L0_attn_in['Wv'], 'L0_attn_Wo': _L0_attn_in['Wo'], 'L0_attn_Wb': _L0_attn_in['Wb'], 'L0_attn_bb': _L0_attn_in['bb'], 'L0_attn_Wd': _L0_attn_in['Wd'], 'L0_attn_bd': _L0_attn_in['bd'], 'L0_ffn_w1': _L0_ffn_in['w1'], 'L0_ffn_w2': _L0_ffn_in['w2'], 'L0_ffn_w3': _L0_ffn_in['w3']}
    _x0 = _d['L0_attn_x']
    _d['L0_attn_x'] = jax.random.normal(jax.random.fold_in(jax.random.key(seed), 1), (2, 1024, 512), dtype=_x0.dtype)
    del _x0
    return _d

def reference(L0_attn_x, L0_attn_Wq, L0_attn_Wk, L0_attn_Wv, L0_attn_Wo, L0_attn_Wb, L0_attn_bb, L0_attn_Wd, L0_attn_bd, L0_ffn_w1, L0_ffn_w2, L0_ffn_w3):

    def _L0_attn_ref(x, Wq, Wk, Wv, Wo, Wb, bb, Wd, bd):
        import jax, jax.numpy as jnp
        import numpy as np
        B, T, D = (8, 1024, 512)
        K, V = (64, 128)

        def _gated_delta(x, Wq, Wk, Wv, Wo, Wb, bb, Wd, bd):
            q = jnp.einsum('btd,dk->btk', x, Wq)
            k = jnp.einsum('btd,dk->btk', x, Wk)
            v = jnp.einsum('btd,dv->btv', x, Wv)
            beta = jax.nn.sigmoid(jnp.einsum('btd,dk->btk', x, Wb) + bb)
            delta = jax.nn.softplus(jnp.einsum('btd,dk->btk', x, Wd) + bd)

            def step(S, inp):
                qt, kt, vt, bt, dt = inp
                kv = jnp.einsum('bk,bv->bkv', kt, vt)
                S = bt[:, :, None] * S + dt[:, :, None] * kv
                ot = jnp.einsum('bk,bkv->bv', qt, S)
                return (S, ot)
            S0 = jnp.zeros((x.shape[0], Wq.shape[1], Wv.shape[1]), dtype=x.dtype)
            xs = tuple((jnp.swapaxes(a, 0, 1) for a in (q, k, v, beta, delta)))
            _, outs = jax.lax.scan(step, S0, xs)
            out = jnp.swapaxes(outs, 0, 1)
            return jnp.einsum('btv,vd->btd', out, Wo)
        return _gated_delta(x, Wq, Wk, Wv, Wo, Wb, bb, Wd, bd)

    def _L0_ffn_ref(x, w1, w2, w3):
        import jax, jax.numpy as jnp
        import numpy as np
        EPS = 1e-08

        def _quantize(w):
            gamma = jnp.mean(jnp.abs(w))
            return jnp.clip(jnp.round(w / (gamma + EPS)), -1.0, 1.0)

        def _bitlinear(x, w):
            return jnp.matmul(x, _quantize(w).T)
        x1 = _bitlinear(x, w1)
        x2 = _bitlinear(x, w2)
        hidden = jax.nn.sigmoid(x1) * x2
        return _bitlinear(hidden, w3)
    x = L0_attn_x
    x = x + _L0_attn_ref(_layernorm(x, axis=-1), L0_attn_Wq, L0_attn_Wk, L0_attn_Wv, L0_attn_Wo, L0_attn_Wb, L0_attn_bb, L0_attn_Wd, L0_attn_bd)
    x = x + _L0_ffn_ref(_layernorm(x, axis=-1), L0_ffn_w1, L0_ffn_w2, L0_ffn_w3)
    return x

_drawn_inputs = setup_inputs


def setup_inputs(seed=0):
    import zlib

    import numpy as np

    out = dict(_drawn_inputs(seed))
    spreads = {}
    factors = {'L0_attn_bb': 4.417, 'L0_attn_bd': 3.057}
    for name, (base, spread) in spreads.items():
        noise = np.random.default_rng([zlib.crc32(name.encode()), seed]).standard_normal(out[name].shape)
        drawn = base * np.exp(spread * noise) if base else spread * noise
        out[name] = jnp.asarray(drawn.astype(out[name].dtype))
    for name, factor in factors.items():
        out[name] = (out[name] * factor).astype(out[name].dtype)
    return out
```

```python
import concourse.bass as bass
from concourse import mybir
from contextlib import ExitStack


class Steps:

    def __init__(self):
        self.before, self.n = 0, 0

    def loop(self, i, per_turn):
        self.entry, self.per_turn = self.before + self.n, per_turn
        self.before, self.n = self.entry + i * per_turn, 0

    def end(self, turns):
        assert self.n == self.per_turn, (self.n, self.per_turn)
        self.before, self.n = self.entry + turns * self.per_turn, 0

    def next(self):
        self.n += 1
        return self.before + self.n


def build_gated_delta_ternary_ffn(nc, x, Wq, Wk, Wv, Wo, Wb, bb, Wd, bd, w1, w2, w3, out):
    f32, f16 = mybir.dt.float32, mybir.dt.float16
    ALU, ACT, AX = mybir.AluOpType, mybir.ActivationFunctionType, mybir.AxisListType

    B, T, D = x.shape
    K, V, H = Wq.shape[1], Wv.shape[1], w1.shape[0]
    P = 128
    C = T // P
    DT, HT = D // P, H // P
    G = C // 2
    NL = 7
    LN_EPS, Q_EPS = 1e-5, 1e-8
    WN = HT * D
    SL = WN // C
    XS = 2048.0
    HS = 64.0
    assert B == 2 and 2 * K == P and V == P and DT == 4 and XS * D ** 0.5 < 65504 and HS * D < 65504

    x_v = x.rearrange("b (c p) d -> p b c d", p=P)
    out_v = out.rearrange("b (c p) d -> p b c d", p=P)
    wn_v = [w.rearrange("(p r) c -> p (r c)", p=P) for w in (w1, w2, w3)]

    ctx = ExitStack()
    with ctx:
        def sb(name, shape, dt=f32):
            return ctx.enter_context(nc.sbuf_tensor(name, shape, dt))

        def pb(name, dt=f32, n=512):
            return ctx.enter_context(nc.psum_tensor(name, [P, n], dt))

        def sem(name):
            return ctx.enter_context(nc.semaphore(name))

        x_sb = sb("x_sb", [P, B, C, D])
        w_nat = sb("w_nat", [P, 3, WN])
        wT = [sb(f"w{n + 1}T", [P, DT, H] if n < 2 else [P, HT, D], f16) for n in range(3)]
        wqk = sb("wqk", [P, DT, 2 * K])
        wbd = sb("wbd", [P, DT, 2 * K])
        wv = sb("wv", [P, DT, V])
        wo = sb("wo", [P, D])
        bias = sb("bias", [P, 2])
        store = sb("store", [P, C, 6 * P])
        cur = sb("cur", [P, 6 * P])
        X = sb("X", [P, NL, 2 * P])
        tot = sb("tot", [P, P])
        tmk = sb("tmk", [P, 2 * 2 * P])
        xn = sb("xn", [P, B, D])
        xnT = sb("xnT", [P, 2, DT, B, P])
        first = sb("first", [P, 11 * P])
        zqb, zkd, sp = (first[:, 2 * n * P:2 * (n + 1) * P].rearrange("p (a n) -> p a n", a=2)
                        for n in range(3))
        e_b, e_d, z_abs, z_pos, z_ln = (first[:, n * P:(n + 1) * P] for n in range(6, 11))
        u_1 = sb("u_1", [P, P])
        stats = sb("stats", [P, B, 6])
        mv = sb("mv", [P, B, 2])
        ve = sb("ve", [P, B])
        rs0 = sb("rs0", [P, B])
        rs1 = sb("rs1", [P, B])
        rs = sb("rs", [P, B])
        rconst = sb("rconst", [P, 6, B])
        idle = sb("idle", [P, 1])
        ident = sb("ident", [P, P])
        ident16 = sb("ident16", [P, P], f16)
        ones = sb("ones", [P, P])
        DIAG, TOP = (NL - 1) * P // 2, (NL + 1) * P // 2
        mask = sb("mask", [P, TOP + P // 2])
        sc = first[:, 0:B * (TOP + P // 2)].rearrange("p (b n) -> p b n", b=B)
        abs_part = sb("abs_part", [P, 3, C])
        abs_sum = sb("abs_sum", [P, 3])
        thr = sb("thr", [P, 2, 3])
        qa = sb("qa", [P, 3, D], f16)
        qn = sb("qn", [P, 3, D], f16)
        GT = sb("GT", [P, P])
        S = sb("S", [P, V])

        w_flat = w_nat[:, :, :].rearrange("p a n -> p (a n)").bitcast(f16)
        xT = w_flat[:, 0:G * 2 * DT * 512].rearrange("p (g s t n) -> p g s t n", g=G, s=2, t=DT)
        hid = w_flat[:, G * 2 * DT * 512:(G * 2 * DT + 2 * HT) * 512].rearrange(
            "p (s j n) -> p s j n", s=2, j=HT)

        w_rest = w_nat[:, :, :].rearrange("p a n -> p (a n)")[:, (G * DT + HT) * 512:]
        sig = w_rest[:, 0:2 * 512].rearrange("p (s n) -> p s n", s=2)
        hid32 = w_rest[:, 2 * 512:4 * 512].rearrange("p (s n) -> p s n", s=2)

        oT = w_rest[:, 2048:2048 + B * P].rearrange("p (b n) -> p b n", b=B)

        bank = [pb(f"ffn{n}") for n in range(3)]
        pa, pb_, pc, pd = pb("pa"), pb("pb"), pb("pc"), pb("pd")
        pe_ = pb("pe")
        pab, pcd = [pa, pb_], [pc, pd]
        abs_out = [w[:, :, :].rearrange("p a n -> p (a n)")[:, 0:SL] for w in wT]
        wbank = [p[:, 0:256].bitcast(f16) for p in bank]

        x_in = [sem("x_even_in"), sem("x_odd_in")]
        w_in = [sem("w_even_in"), sem("w_odd_in")]
        weights_in = sem("weights_in")
        bias_in = sem("bias_in")
        consts, masks_ready = sem("consts"), sem("masks_ready")
        resid_ready = sem("resid_ready")
        pool_steps, dve_steps, act_steps = sem("pool_steps"), sem("dve_steps"), sem("act_steps")
        stats_ready, rstd_ready, xn_ready = sem("stats_ready"), sem("rstd_ready"), sem("xn_ready")
        tile_T = sem("tile_T")
        xnT0_ready, xnT1_ready = sem("xnT0_ready"), sem("xnT1_ready")
        proj_done, v_done, v_stored = sem("proj_done"), sem("v_done"), sem("v_stored")
        z_copied, z_ready, beta_ready, u_ready = (sem("z_copied"), sem("z_ready"), sem("beta_ready"),
                                                  sem("u_ready"))
        stored = sem("stored")
        abs_done, abs_summed, sums_spread = sem("abs_done"), sem("abs_summed"), sem("sums_spread")
        quantised = [sem(f"w{n + 1}_quantised") for n in range(3)]
        w_T = [sem(f"w{n + 1}_T_done") for n in range(3)]
        w_ready = [sem(f"w{n + 1}_ready") for n in range(3)]
        masked = sem("masked")
        cur_ready, chain_ready, levels_done = sem("cur_ready"), sem("chain_ready"), sem("levels_done")
        scores_ready, gt_ready, o_done = sem("scores_ready"), sem("gt_ready"), sem("o_done")
        state_ready, oT_ready, attn_done = sem("state_ready"), sem("oT_ready"), sem("attn_done")
        stats2_ready, rstd2_ready, xn2_ready = sem("stats2_ready"), sem("rstd2_ready"), sem("xn2_ready")
        tile2_T, xhi_ready, xT_ready = sem("tile2_T"), sem("xhi_ready"), sem("xT_ready")
        gate_done, up_done = sem("gate_done"), sem("up_done")
        sig_ready, hid_ready, hi_ready, lo_ready = (sem("sig_ready"), sem("hid_ready"), sem("hi_ready"),
                                                    sem("lo_ready"))
        down_done, y_ready, y_stored = sem("down_done"), sem("y_ready"), sem("y_stored")

        def F(l, rows=slice(0, P)):
            return cur[rows, P:2 * P] if l == 0 else X[rows, l - 1, 0:P]

        def Gk(l, rows=slice(0, P)):
            return cur[rows, 2 * P:3 * P] if l == 0 else X[rows, l - 1, P:2 * P]

        def FG(l):
            return cur[:, P:3 * P] if l == 0 else X[:, l - 1, :]

        def second(ap, l):
            return ap.rearrange("p (n two h) -> p n two h", two=2, h=2 ** l)[:, :, 1, :]

        def level(ap, l):
            return ap.rearrange("p (n h) -> p n h", h=2 ** l)

        off = [0]
        for l in range(NL):
            off.append(off[-1] + P // 2 ** (l + 1))

        def tot_of(l):
            return cur[:, 3 * P:4 * P] if l == 0 else tot[:, off[l - 1]:off[l]]

        UNITS = HT + DT
        PE_AFTER = {"levels": (1, 7), "o": (3, 9), "wo": (4, 10), "t2": (6, 12)}
        DVE_AFTER = {"chain": (0, 6), "masks": (2, 8), "state": (4, 10), "norm2": (5, 11), "xlo": (7, 13)}
        ACT_AFTER = {"gt": (2, 8), "oT": (4, 10), "xhi": (7, 13)}

        def stages(after, u):
            return [(s, k) for k in range(2) for s in after if after[s][k] == u]

        def ahead(i, par, n):
            return i + (par + n) // 2, (par + n) % 2

        starts = {s.name: 1 for s in (
            xn_ready, stored, abs_done, tile_T, xnT0_ready, xnT1_ready, z_copied, v_stored, o_done,
            state_ready, hid_ready, down_done, hi_ready, lo_ready, tile2_T, xT_ready, gt_ready,
            y_ready, *w_T, *w_ready)}
        starts[v_done.name] = 2

        def nth(s, n):
            return n + starts.get(s.name, 0)

        def of(c):
            return bass.ds(c, 1)

        def kept(c, a, b):
            return store[:, of(c), a * P:b * P].rearrange("p o n -> p (o n)")

        def tile(c, b):
            return x_sb[:, b, of(c), :].rearrange("p o n -> p (o n)")

        def xT_part(g, k, b, part):
            return xT[:, of(g), part, :, (2 * k + b) * P:(2 * k + b + 1) * P].rearrange("p o t n -> p (o t) n")

        def tiles(ap):
            return ap.rearrange("p (t n) -> p t n", t=DT)

        def column(l):
            return l * P // 2 if l < NL - 1 else TOP

        def carry_wait():
            nc.vector.memset(idle[:, :], 0.0)

        block = ctx.enter_context(nc.Block())

        @block.sync
        def _(sp_):
            def load_x(i, par):
                for b in range(B):
                    sp_.dma_start(x_sb[:, b, of(2 * i + par), :],
                                  x_v[:, b, of(2 * i + par), :]).then_inc(x_in[par], 16)

            def load_w(i, par):
                for n in range(3):
                    sp_.dma_start(w_nat[:, n, bass.ds((2 * i + par) * SL, SL)],
                                  wn_v[n][:, bass.ds((2 * i + par) * SL, SL)]).then_inc(w_in[par], 16)

            load_x(0, 0)
            for s in (xn_ready, v_done, stored, abs_done, tile_T, xnT0_ready, xnT1_ready, z_copied,
                      v_stored, o_done, state_ready, hid_ready, down_done, hi_ready, lo_ready, tile2_T,
                      xT_ready, gt_ready, y_ready, *w_T, *w_ready):
                sp_.sem_inc(s, starts[s.name])
            for dst, w in ((wqk[:, :, 0:K], Wq), (wqk[:, :, K:2 * K], Wk), (wbd[:, :, 0:K], Wb),
                           (wbd[:, :, K:2 * K], Wd), (wv[:, :, :], Wv)):
                sp_.dma_start(dst, w.rearrange("(t p) k -> p t k", p=P)).then_inc(weights_in, 16)
            load_x(0, 1)
            sp_.dma_start(wo[:, :], Wo).then_inc(weights_in, 16)
            load_w(0, 0)
            load_w(0, 1)
            with sp_.Fori(0, C // 2 - 1) as i:
                for par in range(2):
                    sp_.wait_ge(x_in[par], 32 * (i + 1))
                    load_x(i + 1, par)
                    sp_.wait_ge(w_in[par], 48 * (i + 1))
                    load_w(i + 1, par)

            with sp_.Fori(0, G) as g:
                for m in range(4):
                    sp_.wait_ge(y_ready, nth(y_ready, 4 * g + m + 1))
                    sp_.dma_start(out_v[:, m % 2, of(2 * g + m // 2), :],
                                  x_sb[:, m % 2, of(2 * g + m // 2), :]).then_inc(y_stored, 16)
            sp_.wait_ge(y_stored, 16 * 4 * G)

        @block.gpsimd
        def _(pool):
            st = Steps()

            def link(ins):
                ins.then_inc(pool_steps, 1)
                pool.wait_ge(pool_steps, st.next())

            for b in range(B):
                rows = slice(b * K, (b + 1) * K)
                pool.dma_start(bias[rows, 0:1], bb.rearrange("(k o) -> k o", o=1)).then_inc(bias_in, 16)
                pool.dma_start(bias[rows, 1:2], bd.rearrange("(k o) -> k o", o=1)).then_inc(bias_in, 16)
            nc.gpsimd.memset(ones[:, :], 1.0)
            for n, value in enumerate((LN_EPS, -0.5, -0.5, 1.5, -0.5 * XS, 1.5 * XS)):
                nc.gpsimd.memset(rconst[:, n, :], value)
            nc.gpsimd.memset(tmk[:, :], 1.0)
            nc.gpsimd.memset(S[:, :], 0.0)
            link(nc.gpsimd.memset(ident[:, :], 0.0))
            link(nc.gpsimd.affine_select(out=ident[:, :], in_=ident[:, :], compare_op=ALU.not_equal,
                                             fill=1.0, base=0, pattern=[[-1, P]], channel_multiplier=1))
            nc.gpsimd.tensor_copy(ident16[:, :], ident[:, :]).then_inc(consts, 1)

            def make_masks():
                nc.gpsimd.tensor_copy(mask[:, DIAG:DIAG + P], ident[:, :])
                for l in range(NL):
                    h, n = 2 ** l, P // 2 ** (l + 1)
                    m = level(mask[:, column(l):column(l) + P // 2], l)
                    link(nc.gpsimd.affine_select(out=m, in_=level(ones[:, 0:P // 2], l),
                                                     compare_op=ALU.is_ge, fill=0.0, base=0,
                                                     pattern=[[-2 * h, n], [0, h]], channel_multiplier=1))
                    last = nc.gpsimd.affine_select(out=m, in_=m, compare_op=ALU.is_gt, fill=0.0, base=h,
                                                   pattern=[[2 * h, n], [0, h]], channel_multiplier=-1)
                last.then_inc(masks_ready, 1)

            def rstd(scale, out_sem):
                k = 2 if scale == 1.0 else 4

                def op(out, a, b, alu):
                    return nc.gpsimd.tensor_tensor(out[:, :], a, b, alu)
                link(op(ve, mv[:, :, 1], rconst[:, 0, :], ALU.add))
                link(op(rs0, ve[:, :], rconst[:, 1, :], ALU.pow))
                link(op(rs1, rs0[:, :], rs0[:, :], ALU.mult))
                link(op(rs1, rs1[:, :], ve[:, :], ALU.mult))
                link(op(rs1, rs1[:, :], rconst[:, k, :], ALU.mult))
                link(op(rs1, rs1[:, :], rconst[:, k + 1, :], ALU.add))
                op(rs, rs1[:, :], rs0[:, :], ALU.mult).then_inc(out_sem, 1)
            RSTD_STEPS, GATE_STEPS = 6, 2

            def norm(i, par):
                c = 2 * i + par
                pool.wait_ge(stats_ready, c + 1)
                pool.wait_ge(xn_ready, nth(xn_ready, c))
                rstd(1.0, rstd_ready)

            def gates(i, par):
                c = 2 * i + par
                pool.wait_ge(z_ready, c + 1)
                pool.wait_ge(u_ready, c + 1)
                nc.gpsimd.tensor_tensor(sp[:, 0, :], u_1[:, :], e_d[:, :], ALU.subtract)
                link(nc.gpsimd.tensor_tensor(sp[:, 1, :], z_pos[:, :], z_ln[:, :], ALU.add))
                link(nc.gpsimd.tensor_tensor(sp[:, 1, :], sp[:, 1, :], sp[:, 0, :], ALU.subtract))
                nc.gpsimd.tensor_tensor(kept(c, 2, 3), sp[:, 1, :], zkd[:, 0, :], ALU.mult)
                nc.gpsimd.tensor_copy(kept(c, 0, 1), zqb[:, 0, :])
                pool.wait_ge(beta_ready, c + 1)
                nc.gpsimd.tensor_tensor(kept(c, 1, 2), zqb[:, 0, :], kept(c, 3, 4),
                                        ALU.mult).then_inc(stored, 1)

            norm(0, 0)
            norm(0, 1)
            with pool.Fori(0, C // 2 - 1) as i:
                st.loop(i, 2 * (RSTD_STEPS + GATE_STEPS))
                for par in range(2):
                    norm(i + 1, par)
                    gates(i, par)
                st.end(C // 2 - 1)
            gates(C // 2 - 1, 0)
            gates(C // 2 - 1, 1)
            make_masks()

            def fetch(c):
                pool.wait_ge(o_done, nth(o_done, c))
                pool.wait_ge(state_ready, nth(state_ready, c))
                nc.gpsimd.tensor_copy(cur[:, :], kept(c, 0, 6)).then_inc(cur_ready, 1)

            def join(c):
                pool.wait_ge(masked, c + 1)
                for l in range(NL):
                    a = sc[:, :, DIAG:DIAG + P].rearrange("p b (n two h) -> p b n two h", two=2, h=2 ** l)[
                        :, :, :, 1, :]
                    last = nc.gpsimd.tensor_tensor(
                        a, a, sc[:, :, column(l):column(l) + P // 2].rearrange("p b (n h) -> p b n h", h=2 ** l),
                        ALU.add)
                    if l < NL - 1:
                        link(last)
                last.then_inc(scores_ready, 1)

            def norm2(c):
                pool.wait_ge(stats2_ready, c + 1)
                rstd(XS, rstd2_ready)

            pool.wait_ge(v_stored, nth(v_stored, C))
            for c in range(2):
                fetch(c)
                join(c)
                norm2(c)
            with pool.Fori(0, G - 1) as g:
                st.loop(g, 2 * (RSTD_STEPS + NL - 1))
                for k in range(2):
                    fetch(2 * g + 2 + k)
                    join(2 * g + 2 + k)
                    norm2(2 * g + 2 + k)
                st.end(G - 1)

        @block.scalar
        def _(act):
            st = Steps()

            def link(ins):
                ins.then_inc(act_steps, 1)
                act.wait_ge(act_steps, st.next())

            act.wait_ge(bias_in, 64)
            link(nc.scalar.activation(bias[:, 0:1], bias[:, 0:1], ACT.Copy, scale=-1.0))

            def evacuate_T(i, par):
                c = 2 * i + par
                act.wait_ge(tile_T, nth(tile_T, 2 * c + 1))
                act.wait_ge(v_done, nth(v_done, c - 1))
                nc.scalar.activation(xnT[:, par, :, 0, :], tiles(pa[:, :]), ACT.Copy).then_inc(xnT0_ready, 1)

            def exps(i, par):
                c = 2 * i + par
                act.wait_ge(stored, nth(stored, c))
                act.wait_ge(proj_done, c + 1)
                z = pc[:, :].rearrange("p (a b n) -> p a b n", a=2, b=B)
                for b in range(B):
                    rows = slice(b * K, (b + 1) * K)
                    nc.scalar.activation(zqb[rows, :, :], z[0:K, :, b, :], ACT.Copy)
                    last = nc.scalar.activation(zkd[rows, :, :], z[K:2 * K, :, b, :], ACT.Copy)
                last.then_inc(z_copied, 1)
                act.wait_ge(z_copied, nth(z_copied, c + 1))
                nc.scalar.activation(z_abs[:, :], zkd[:, 1, :], ACT.Abs, bias=bias[:, 1:2])
                nc.scalar.activation(z_pos[:, :], zkd[:, 1, :], ACT.Relu, bias=bias[:, 1:2])
                link(nc.scalar.activation(e_b[:, :], zqb[:, 1, :], ACT.Exp, scale=-1.0,
                                              bias=bias[:, 0:1]))
                link(nc.scalar.activation(e_d[:, :], z_abs[:, :], ACT.Exp, scale=-1.0))
                nc.scalar.activation(z_ln[:, :], e_d[:, :], ACT.Ln, bias=ones[:, 0:1]).then_inc(z_ready, 1)

            def absum(i, par):
                c = 2 * i + par
                act.wait_ge(w_in[par], 48 * (i + 1))
                act.wait_ge(abs_done, nth(abs_done, c))
                for n in range(3):
                    last = nc.scalar.activation(abs_out[n], w_nat[:, n, bass.ds(c * SL, SL)], ACT.Abs,
                                                accum_out=abs_part[:, n, of(c)])
                last.then_inc(abs_done, 1)

            act.wait_ge(consts, 1)
            evacuate_T(0, 0)
            with act.Fori(0, C // 2 - 1) as i:
                st.loop(i, 4)
                for par in range(2):
                    evacuate_T(*ahead(i, par, 1))
                    exps(i, par)
                    absum(i, par)
                st.end(C // 2 - 1)
            evacuate_T(C // 2 - 1, 1)
            exps(C // 2 - 1, 0)
            absum(C // 2 - 1, 0)
            absum(C // 2 - 1, 1)
            exps(C // 2 - 1, 1)

            with act.Fori(0, HT) as j:
                for n in range(3):
                    act.wait_ge(w_T[n], nth(w_T[n], j + 1))
                    if n < 2:
                        dst = wT[n][:, :, bass.ds(j * P, P)]
                    else:
                        dst = wT[2][:, of(j), :].rearrange("p o (n t) -> p (o t) n", t=DT)
                    nc.scalar.activation(dst, tiles(wbank[n]), ACT.Copy).then_inc(w_ready[n], 1)

            def attn(s, g, k):
                c = 2 * g + k
                if s == "gt":
                    act.wait_ge(levels_done, c + 1)
                    nc.scalar.activation(GT[:, :], pe_[:, 0:P], ACT.Copy).then_inc(gt_ready, 1)
                if s == "oT":
                    act.wait_ge(o_done, nth(o_done, c + 1))
                    for b in range(B):
                        last = nc.scalar.activation(oT[:, b, :], pcd[b][:, 0:P], ACT.Copy)
                    last.then_inc(oT_ready, 1)
                if s == "xhi":
                    for b in range(B):
                        act.wait_ge(tile2_T, nth(tile2_T, 2 * c + b + 1))
                        nc.scalar.activation(xT_part(g, k, b, 0), tiles(pcd[b][:, :]),
                                             ACT.Copy).then_inc(xhi_ready, 1)

            for n in range(3):
                act.wait_ge(quantised[n], HT)
            for k in range(2):
                for s in ("gt", "oT", "xhi"):
                    attn(s, 0, k)

            def group(g, work):
                for u in range(UNITS):
                    if u < HT:
                        act.wait_ge(gate_done, g * HT + u + 1)
                        act.wait_ge(hid_ready, nth(hid_ready, g * HT + max(u - 1, 0)))
                        nc.scalar.activation(sig[:, u % 2, :], bank[2 * u % 3][:, :], ACT.Sigmoid,
                                             scale=-1.0 / XS).then_inc(sig_ready, 1)
                    if 1 <= u <= HT:
                        act.wait_ge(hid_ready, nth(hid_ready, g * HT + u))
                        if u == 1:
                            act.wait_ge(down_done, nth(down_done, g * DT))
                        nc.scalar.activation(hid[:, 0, u - 1, :], hid32[:, (u - 1) % 2, :],
                                             ACT.Copy).then_inc(hi_ready, 1)
                    if work:
                        for s, k in stages(ACT_AFTER, u):
                            attn(s, g + 1, k)

            with act.Fori(0, G - 1) as g:
                group(g, True)
            group(G - 1, False)

        @block.vector
        def _(dve):
            st = Steps()

            def link(ins):
                ins.then_inc(dve_steps, 1)
                dve.wait_ge(dve_steps, st.next())


            def statistics(c, out_sem):
                carry_wait()
                for b in range(B):
                    last = nc.vector.bn_stats(stats[:, b, :], tile(c, b))
                link(last)
                carry_wait()
                for b in range(B):
                    last = nc.vector.bn_aggr(mv[:, b, :], stats[:, b, :])
                last.then_inc(out_sem, 1)

            def normalise(c, out_sem):
                for b in range(B):
                    last = nc.vector.tensor_scalar(xn[:, b, :], tile(c, b), mv[:, b, 0:1], rs[:, b:b + 1],
                                                   ALU.subtract, ALU.mult)
                last.then_inc(out_sem, 1)

            def norm(i, par):
                c = 2 * i + par
                dve.wait_ge(x_in[par], 32 * (i + 1))
                dve.wait_ge(xn_ready, nth(xn_ready, c))
                statistics(c, stats_ready)
                dve.wait_ge(rstd_ready, c + 1)
                dve.wait_ge(tile_T, nth(tile_T, 2 * c))
                normalise(c, xn_ready)

            def evacuate_T(i, par):
                c = 2 * i + par
                dve.wait_ge(tile_T, nth(tile_T, 2 * c + 2))
                dve.wait_ge(v_done, nth(v_done, c - 1))
                nc.vector.tensor_copy(xnT[:, par, :, 1, :], tiles(pb_[:, :])).then_inc(xnT1_ready, 1)

            def gates(i, par):
                c = 2 * i + par
                dve.wait_ge(v_done, nth(v_done, c + 1))
                nc.vector.tensor_copy(kept(c, 4, 6), pd[:, 0:B * V]).then_inc(v_stored, 1)
                dve.wait_ge(z_ready, c + 1)
                nc.vector.tensor_scalar(u_1[:, :], e_d[:, :], 1.0, -1.0, ALU.add, ALU.add).then_inc(u_ready, 1)
                link(nc.vector.tensor_scalar(e_b[:, :], e_b[:, :], 1.0, None, ALU.add))
                nc.vector.reciprocal(kept(c, 3, 4), e_b[:, :]).then_inc(beta_ready, 1)

            norm(0, 0)
            evacuate_T(0, 0)
            norm(0, 1)
            with dve.Fori(0, C // 2 - 1) as i:
                st.loop(i, 4)
                for par in range(2):
                    evacuate_T(*ahead(i, par, 1))
                    norm(i + 1, par)
                    gates(i, par)
                st.end(C // 2 - 1)
            evacuate_T(C // 2 - 1, 1)
            gates(C // 2 - 1, 0)
            gates(C // 2 - 1, 1)

            dve.wait_ge(abs_done, nth(abs_done, C))
            nc.vector.tensor_reduce(abs_sum[:, :], abs_part[:, :, :], AX.X, ALU.add).then_inc(abs_summed, 1)
            dve.wait_ge(sums_spread, 1)
            link(nc.vector.tensor_scalar(thr[:, 0, :], pe_[:, 0:3], 0.5 / (H * D), 0.5 * Q_EPS,
                                             ALU.mult, ALU.add))
            link(nc.vector.tensor_scalar(thr[:, 1, :], thr[:, 0, :], -1.0, None, ALU.mult))

            with dve.Fori(0, HT) as j:
                st.loop(j, 3)
                for n in range(3):
                    if n < 2:
                        piece = tiles(w_nat[:, n, bass.ds(j * D, D)])
                    else:
                        piece = w_nat[:, 2, :].rearrange("p (t q r) -> p t q r", t=DT, r=HT)[
                            :, :, :, of(j)].rearrange("p t q o -> p t (q o)")
                    link(nc.vector.tensor_scalar(tiles(qa[:, n, :]), piece, thr[:, 0, n:n + 1], None,
                                                     ALU.is_gt))
                    dve.wait_ge(w_T[n], nth(w_T[n], j))
                    nc.vector.scalar_tensor_tensor(tiles(qn[:, n, :]), piece, thr[:, 1, n:n + 1],
                                                   tiles(qa[:, n, :]), ALU.is_lt,
                                                   ALU.subtract).then_inc(quantised[n], 1)
                st.end(HT)

            def chain(c):
                dve.wait_ge(cur_ready, c + 1)
                for l in range(NL):
                    n, h = P // 2 ** (l + 1), 2 ** l
                    t = tot_of(l).rearrange("p (n two) -> p n two", two=2)
                    m = tmk[:, 0:4 * n].rearrange("p (a n two) -> p a n two", a=2, two=2)
                    nc.vector.tensor_copy(m[:, 0, :, 1], t[:, :, 0])
                    nc.vector.tensor_copy(m[:, 1, :, 0], t[:, :, 1])
                    nc.vector.memset(m[:, 0, :, 0], 1.0)
                    nc.vector.memset(m[:, 1, :, 1], 1.0)
                    link(nc.vector.tensor_tensor(tot_of(l + 1), t[:, :, 0], t[:, :, 1], ALU.mult))
                    last = nc.vector.tensor_tensor(
                        FG(l + 1).rearrange("p (n h) -> p n h", h=h),
                        FG(l).rearrange("p (n h) -> p n h", h=h),
                        tmk[:, 0:4 * n].unsqueeze(2).broadcast_to([P, 4 * n, h]), ALU.mult)
                    if l < NL - 1:
                        link(last)
                last.then_inc(chain_ready, 1)
            CHAIN_STEPS = 2 * NL - 1

            def attn(s, g, k):
                c = 2 * g + k
                if s == "chain":
                    chain(c)
                if s == "masks":
                    dve.wait_ge(levels_done, c + 1)
                    for b in range(B):
                        nc.vector.tensor_tensor(sc[:, b, 0:TOP], pab[b][:, :], mask[:, 0:TOP], ALU.mult)
                        last = nc.vector.tensor_tensor(sc[:, b, TOP:TOP + P // 2], pcd[b][:, 0:P // 2],
                                                       mask[:, TOP:TOP + P // 2], ALU.mult)
                    last.then_inc(masked, 1)
                if s == "state":
                    dve.wait_ge(o_done, nth(o_done, c + 1))
                    nc.vector.scalar_tensor_tensor(S[:, :], S[:, :], tot_of(NL), pe_[:, 0:V], ALU.mult,
                                                   ALU.add).then_inc(state_ready, 1)
                if s == "norm2":
                    dve.wait_ge(attn_done, c + 1)
                    for b in range(B):
                        last = nc.vector.tensor_tensor(tile(c, b), tile(c, b), pab[b][:, :], ALU.add)
                    last.then_inc(resid_ready, 1)
                    dve.wait_ge(resid_ready, c + 1)
                    statistics(c, stats2_ready)
                    dve.wait_ge(rstd2_ready, c + 1)
                    dve.wait_ge(tile2_T, nth(tile2_T, 2 * c))
                    normalise(c, xn2_ready)
                if s == "xlo":
                    for b in range(B):
                        dve.wait_ge(xhi_ready, 2 * c + b + 1)
                        nc.vector.tensor_tensor(xT_part(g, k, b, 1), tiles(pcd[b][:, :]),
                                                xT_part(g, k, b, 0), ALU.subtract).then_inc(xT_ready, 1)
            ATTN_STEPS = CHAIN_STEPS + 1

            dve.wait_ge(masks_ready, 1)
            for k in range(2):
                for s in DVE_AFTER:
                    attn(s, 0, k)

            def group(g, work):
                for u in range(UNITS):
                    if u < HT:
                        dve.wait_ge(up_done, g * HT + u + 1)
                        dve.wait_ge(sig_ready, g * HT + u + 1)
                        dve.wait_ge(hi_ready, nth(hi_ready, g * HT + max(u - 1, 0)))
                        dve.wait_ge(lo_ready, nth(lo_ready, g * HT + max(u - 1, 0)))
                        nc.vector.scalar_tensor_tensor(hid32[:, u % 2, :], bank[(2 * u + 1) % 3][:, :],
                                                       HS / XS, sig[:, u % 2, :], ALU.mult,
                                                       ALU.mult).then_inc(hid_ready, 1)
                    if 1 <= u <= HT:
                        dve.wait_ge(hi_ready, nth(hi_ready, g * HT + u))
                        nc.vector.tensor_tensor(hid[:, 1, u - 1, :], hid32[:, (u - 1) % 2, :],
                                                hid[:, 0, u - 1, :], ALU.subtract).then_inc(lo_ready, 1)
                    if u >= HT:
                        m = u - HT
                        dve.wait_ge(down_done, nth(down_done, g * DT + m + 1))
                        y = tile(2 * g + m // 2, m % 2)
                        nc.vector.scalar_tensor_tensor(y, bank[(2 * HT + m) % 3][:, :], 1.0 / HS, y, ALU.mult,
                                                       ALU.add).then_inc(y_ready, 1)
                    if work:
                        for s, k in stages(DVE_AFTER, u):
                            attn(s, g + 1, k)

            with dve.Fori(0, G - 1) as g:
                st.loop(g, 2 * ATTN_STEPS)
                group(g, True)
                st.end(G - 1)
            group(G - 1, False)

        @block.tensor
        def _(pe):
            pe.wait_ge(consts, 1)

            def transposes(i, par):
                c = 2 * i + par
                pe.wait_ge(xn_ready, nth(xn_ready, c + 1))
                pe.wait_ge(xnT0_ready, nth(xnT0_ready, c))
                pe.wait_ge(xnT1_ready, nth(xnT1_ready, c))
                for b in range(B):
                    for t in range(DT):
                        last = nc.tensor.transpose(pab[b][:, t * P:(t + 1) * P], xn[:, b, t * P:(t + 1) * P],
                                                   ident[:, :])
                    last.then_inc(tile_T, 1)

            def project(i, par):
                c = 2 * i + par
                pe.wait_ge(xnT0_ready, nth(xnT0_ready, c + 1))
                pe.wait_ge(xnT1_ready, nth(xnT1_ready, c + 1))
                pe.wait_ge(z_copied, nth(z_copied, c))
                for a, w in enumerate((wqk, wbd)):
                    for t in range(DT):
                        last = nc.tensor.matmul(pc[:, a * 256:(a + 1) * 256], w[:, t, :], xnT[:, par, t, :, :],
                                                start=t == 0, stop=t == DT - 1)
                last.then_inc(proj_done, 1)
                pe.wait_ge(v_stored, nth(v_stored, c))
                for b in range(B):
                    for t in range(DT):
                        last = nc.tensor.matmul(pd[:, b * V:(b + 1) * V], xnT[:, par, t, b, :], wv[:, t, :],
                                                start=t == 0, stop=t == DT - 1)
                last.then_inc(v_done, 1)

            transposes(0, 0)
            pe.wait_ge(weights_in, 16 * 6)
            with pe.Fori(0, C // 2 - 1) as i:
                for par in range(2):
                    transposes(*ahead(i, par, 1))
                    project(i, par)
            transposes(C // 2 - 1, 1)
            project(C // 2 - 1, 0)
            project(C // 2 - 1, 1)

            pe.wait_ge(abs_summed, 1)
            nc.tensor.matmul(pe_[:, 0:3], ones[:, :], abs_sum[:, :], start=True, stop=True
                             ).then_inc(sums_spread, 1)
            with pe.Fori(0, HT) as j:
                for n in range(3):
                    pe.wait_ge(quantised[n], j + 1)
                    pe.wait_ge(w_ready[n], nth(w_ready[n], j))
                    for t in range(DT):
                        last = nc.tensor.transpose(wbank[n][:, t * P:(t + 1) * P],
                                                   qn[:, n, t * P:(t + 1) * P], ident16[:, :])
                    last.then_inc(w_T[n], 1)

            def attn(s, g, k):
                c = 2 * g + k
                half = [slice(b * K, (b + 1) * K) for b in range(B)]
                if s == "levels":
                    pe.wait_ge(chain_ready, c + 1)
                    pe.wait_ge(xT_ready, nth(xT_ready, 2 * c))
                    pe.wait_ge(gt_ready, nth(gt_ready, c))
                    for l in range(NL):
                        for b in range(B):
                            dst = (pab[b][:, column(l):column(l) + P // 2] if l < NL - 1
                                   else pcd[b][:, 0:P // 2])
                            nc.tensor.matmul(dst, Gk(l, half[b]), second(F(l, half[b]), l), start=True, stop=True)
                    for b in range(B):
                        nc.tensor.matmul(pab[b][:, DIAG:DIAG + P], Gk(0, half[b]), cur[half[b], 0:P],
                                         start=True, stop=True)
                    nc.tensor.transpose(pe_[:, 0:P], Gk(NL), ident[:, :]).then_inc(levels_done, 1)
                if s == "o":
                    pe.wait_ge(scores_ready, c + 1)
                    pe.wait_ge(gt_ready, nth(gt_ready, c + 1))
                    pe.wait_ge(state_ready, nth(state_ready, c))
                    for b in range(B):
                        o = pcd[b][:, 0:P]
                        v = cur[:, (4 + b) * P:(5 + b) * P]
                        nc.tensor.matmul(o, v, sc[:, b, DIAG:DIAG + P], start=True, stop=False)
                        nc.tensor.matmul(o, S[half[b], :], F(NL, half[b]), start=False, stop=True)
                    for b in range(B):
                        v = cur[:, (4 + b) * P:(5 + b) * P]
                        last = nc.tensor.matmul(pe_[half[b], 0:V], GT[:, half[b]], v, start=True, stop=True)
                    last.then_inc(o_done, 1)
                if s == "wo":
                    pe.wait_ge(oT_ready, c + 1)
                    for b in range(B):
                        last = nc.tensor.matmul(pab[b][:, :], oT[:, b, :], wo[:, :], start=True, stop=True)
                    last.then_inc(attn_done, 1)
                if s == "t2":
                    pe.wait_ge(xn2_ready, c + 1)
                    pe.wait_ge(oT_ready, c + 1)
                    for b in range(B):
                        for t in range(DT):
                            last = nc.tensor.transpose(pcd[b][:, t * P:(t + 1) * P],
                                                       xn[:, b, t * P:(t + 1) * P], ident[:, :])
                        last.then_inc(tile2_T, 1)

            for k in range(2):
                for s in PE_AFTER:
                    attn(s, 0, k)

            def bank_free(g, n):
                m = n - 3
                if m < 0:
                    return
                if m < 2 * HT:
                    pe.wait_ge(hid_ready if m % 2 else sig_ready, nth(hid_ready if m % 2 else sig_ready, g * HT + m // 2 + 1))
                else:
                    pe.wait_ge(y_ready, nth(y_ready, g * DT + m - 2 * HT + 1))

            def group(g, work):
                for n in range(3):
                    pe.wait_ge(w_ready[n], nth(w_ready[n], HT))
                pe.wait_ge(xT_ready, nth(xT_ready, 4 * g + 4))
                pe.wait_ge(y_ready, nth(y_ready, g * DT))
                for u in range(UNITS):
                    if u < HT:
                        for a in range(2):
                            n = 2 * u + a
                            bank_free(g, n)
                            for t in range(DT):
                                for part in range(2):
                                    last = nc.tensor.matmul(
                                        bank[n % 3][:, :], wT[a][:, t, u * P:(u + 1) * P],
                                        xT[:, of(g), part, t, :].rearrange("p o n -> p (o n)"),
                                        start=t == 0 and part == 0, stop=t == DT - 1 and part == 1)
                            last.then_inc((gate_done, up_done)[a], 1)
                    else:
                        m = u - HT
                        bank_free(g, 2 * HT + m)
                        for part in range(2):
                            for j in range(HT):
                                if m == 0:
                                    pe.wait_ge((hi_ready, lo_ready)[part], nth((hi_ready, lo_ready)[part], g * HT + j + 1))
                                last = nc.tensor.matmul(bank[(2 * HT + m) % 3][:, :],
                                                        hid[:, part, j, m * P:(m + 1) * P], wT[2][:, j, :],
                                                        start=part == 0 and j == 0,
                                                        stop=part == 1 and j == HT - 1)
                        last.then_inc(down_done, 1)
                    if work:
                        for s, k in stages(PE_AFTER, u):
                            attn(s, g + 1, k)

            with pe.Fori(0, G - 1) as g:
                group(g, True)
            group(G - 1, False)


_INS = ['L0_attn_x', 'L0_attn_Wq', 'L0_attn_Wk', 'L0_attn_Wv', 'L0_attn_Wo', 'L0_attn_Wb', 'L0_attn_bb',
        'L0_attn_Wd', 'L0_attn_bd', 'L0_ffn_w1', 'L0_ffn_w2', 'L0_ffn_w3']


def kernel(**inputs):
    import numpy as _np
    import concourse.bacc as _bacc
    from concourse import mybir as _mybir
    from concourse.bass_utils import run_bass_kernel_spmd as _run

    nc = _bacc.Bacc("TRN2", target_bir_lowering=False, num_devices=1)
    arrays, args = {}, []
    for name in _INS:
        a = _np.ascontiguousarray(inputs[name])
        arrays[f"in_{name}_dram"] = a
        args.append(nc.dram_tensor(f"in_{name}_dram", a.shape, _mybir.dt.from_np(a.dtype),
                                   kind="ExternalInput").ap())
    x = inputs['L0_attn_x']
    out = nc.dram_tensor("out_0_dram", x.shape, _mybir.dt.float32, kind="ExternalOutput").ap()
    build_gated_delta_ternary_ffn(nc, *args, out)
    r = _run(nc, [arrays], core_ids=[0])
    return r.results[0]["out_0_dram"]
```

```python
import concourse.bass as bass
from concourse import mybir
from contextlib import ExitStack


class Steps:

    def __init__(self):
        self.before, self.n = 0, 0

    def loop(self, i, per_turn):
        self.entry, self.per_turn = self.before + self.n, per_turn
        self.before, self.n = self.entry + i * per_turn, 0

    def end(self, turns):
        assert self.n == self.per_turn, (self.n, self.per_turn)
        self.before, self.n = self.entry + turns * self.per_turn, 0

    def next(self):
        self.n += 1
        return self.before + self.n


def build_gated_delta_ternary_ffn(nc, x, Wq, Wk, Wv, Wo, Wb, bb, Wd, bd, w1, w2, w3, out):
    f32, f16 = mybir.dt.float32, mybir.dt.float16
    ALU, ACT, AX = mybir.AluOpType, mybir.ActivationFunctionType, mybir.AxisListType

    B, T, D = x.shape
    K, V, H = Wq.shape[1], Wv.shape[1], w1.shape[0]
    P = 128
    C = T // P
    DT, HT = D // P, H // P
    G = C // 2
    NL = 7
    LN_EPS, Q_EPS = 1e-5, 1e-8
    WN = HT * D
    SL = WN // C
    XS = 2048.0
    HS = 64.0
    assert B == 2 and 2 * K == P and V == P and DT == 4 and XS * D ** 0.5 < 65504 and HS * D < 65504

    x_v = x.rearrange("b (c p) d -> p b c d", p=P)
    out_v = out.rearrange("b (c p) d -> p b c d", p=P)
    wn_v = [w.rearrange("(p r) c -> p (r c)", p=P) for w in (w1, w2, w3)]

    ctx = ExitStack()
    with ctx:
        def sb(name, shape, dt=f32):
            return ctx.enter_context(nc.sbuf_tensor(name, shape, dt))

        def pb(name, dt=f32, n=512):
            return ctx.enter_context(nc.psum_tensor(name, [P, n], dt))

        def sem(name):
            return ctx.enter_context(nc.semaphore(name))

        x_sb = sb("x_sb", [P, B, C, D])
        XT = DT * 512
        w_nat = sb("w_nat", [P, 3 * WN + XT])
        nat = [w_nat[:, at:at + WN] for at in (0, WN + XT, 2 * WN + XT)]
        wT = [sb(f"w{n + 1}T", [P, DT, H] if n < 2 else [P, HT, D], f16) for n in range(3)]
        wqk = sb("wqk", [P, DT, 2 * K])
        wbd = sb("wbd", [P, DT, 2 * K])
        wv = sb("wv", [P, DT, V])
        wo = sb("wo", [P, D])
        bias = sb("bias", [P, 2])
        store = sb("store", [P, C, 6 * P])
        cur = sb("cur", [P, 8 * P])
        X = sb("X", [P, NL, 3 * P])
        tot = sb("tot", [P, P])
        tmk = sb("tmk", [P, 3 * 2 * P])
        xn = sb("xn", [P, B, D])
        xn2 = sb("xn2", [P, B, D])
        xnT = sb("xnT", [P, 2, DT, B, P])
        first = wT[2][:, HT - 6:HT, :].rearrange("p a n -> p (a n)").bitcast(f32)
        zqb, zkd, sp = (first[:, 2 * n * P:2 * (n + 1) * P].rearrange("p (a n) -> p a n", a=2)
                        for n in range(3))
        e_b, e_d, z_abs, z_pos, z_ln = (first[:, n * P:(n + 1) * P] for n in range(6, 11))
        u_1 = first[:, 11 * P:12 * P]
        stats, stats2 = sb("stats", [P, B, 6]), sb("stats2", [P, B, 6])
        mv, mv2 = sb("mv", [P, B, 2]), sb("mv2", [P, B, 2])
        ve, rs0, rs1 = sb("ve", [P, B]), sb("rs0", [P, B]), sb("rs1", [P, B])
        rs, rs2 = sb("rs", [P, B]), sb("rs2", [P, B])
        rconst = sb("rconst", [P, 6, B])
        idle = sb("idle", [P, 1])
        ident = sb("ident", [P, P])
        pos16, neg16 = sb("pos16", [P, P], f16), sb("neg16", [P, P], f16)
        ones = sb("ones", [P, P])
        mask = sb("mask", [P, NL, P // 2])
        DIAG = NL * P
        sc = sb("sc", [P, DIAG + 2 * P])
        abs_part = sb("abs_part", [P, 3, C])
        abs_sum = sb("abs_sum", [P, 3])
        thr = sb("thr", [P, 2, 3])
        above, below = sb("above", [P, 3, D], f16), sb("below", [P, 3, D], f16)
        GT = sb("GT", [P, P])
        S = sb("S", [P, V])
        oT = sb("oT", [P, B, P])

        hid = w_nat[:, 0:WN].bitcast(f16).rearrange("p (j s n) -> p s j n", s=2, j=HT)
        xT = w_nat[:, WN:WN + G * XT].bitcast(f16).rearrange("p (g s t n) -> p g s t n", g=G, s=2, t=DT)
        late = xnT[:, :, :, :, :].rearrange("p a t b n -> p (a t b n)")
        sig = late[:, 0:2 * 512].rearrange("p (s n) -> p s n", s=2)
        hid32 = late[:, 2 * 512:4 * 512].rearrange("p (s n) -> p s n", s=2)

        bank = [pb(f"ffn{n}") for n in range(3)]
        pa, pb_, pc, pe_, pd = pb("pa"), pb("pb"), pb("pc"), pb("pe"), pb("pd")
        pab = [pa, pb_]
        abs_out = [w[:, :, :].rearrange("p a n -> p (a n)")[:, 0:SL] for w in wT]

        x_in = [sem("x_even_in"), sem("x_odd_in")]
        w_in = [sem("w_even_in"), sem("w_odd_in")]
        weights_in, wo_in = sem("weights_in"), sem("wo_in")
        bias_in = sem("bias_in")
        consts = sem("consts")
        resid_ready = sem("resid_ready")
        pool_steps, dve_steps, act_steps = sem("pool_steps"), sem("dve_steps"), sem("act_steps")
        stats_ready, rstd_ready, xn_ready = sem("stats_ready"), sem("rstd_ready"), sem("xn_ready")
        tile_T = sem("tile_T")
        xnT0_ready, xnT1_ready = sem("xnT0_ready"), sem("xnT1_ready")
        proj_done, v_done, v_stored = sem("proj_done"), sem("v_done"), sem("v_stored")
        z_copied, z_ready, beta_ready, u_ready = (sem("z_copied"), sem("z_ready"), sem("beta_ready"),
                                                  sem("u_ready"))
        stored = sem("stored")
        abs_done, abs_summed, sums_spread = sem("abs_done"), sem("abs_summed"), sem("sums_spread")
        quantised, w_T, w_ready = sem("quantised"), sem("w_T"), sem("w_ready")
        masked, factors_ready, gbv_ready = sem("masked"), sem("factors_ready"), sem("gbv_ready")
        cur_ready, chain_ready, levels_done = sem("cur_ready"), sem("chain_ready"), sem("levels_done")
        scores_ready, gt_ready, o_done = sem("scores_ready"), sem("gt_ready"), sem("o_done")
        state_ready, oT_ready, attn_done = sem("state_ready"), sem("oT_ready"), sem("attn_done")
        stats2_ready, rstd2_ready, xn2_ready = sem("stats2_ready"), sem("rstd2_ready"), sem("xn2_ready")
        tile2_T, xhi_ready, xT_ready = sem("tile2_T"), sem("xhi_ready"), sem("xT_ready")
        gate_done, up_done = sem("gate_done"), sem("up_done")
        sig_ready, hid_ready, hi_ready, lo_ready = (sem("sig_ready"), sem("hid_ready"), sem("hi_ready"),
                                                    sem("lo_ready"))
        down_done, y_ready, y_stored = sem("down_done"), sem("y_ready"), sem("y_stored")

        def F(l):
            return cur[:, 2 * P:4 * P] if l == 0 else X[:, l - 1, 0:2 * P]

        def Gk(l):
            return cur[:, 4 * P:5 * P] if l == 0 else X[:, l - 1, 2 * P:3 * P]

        def FG(l):
            return cur[:, 2 * P:5 * P] if l == 0 else X[:, l - 1, :]

        def second(ap, l):
            return ap.rearrange("p (b n two h) -> p b n two h", b=B, two=2, h=2 ** l)[:, :, :, 1, :]

        def level(ap, l):
            return ap.rearrange("p (n h) -> p n h", h=2 ** l)

        off = [0]
        for l in range(NL):
            off.append(off[-1] + P // 2 ** (l + 1))

        def tot_of(l):
            return tot[:, off[l - 1]:off[l]]

        def factors(l):
            n = P // 2 ** (l + 1)
            at = 3 * (2 * P - P // 2 ** l * 2)
            return tmk[:, at:at + 6 * n]

        UNITS = HT + DT
        PE_AFTER = {"levels": (2, 8), "o": (4, 10), "wo": (5, 11), "t2": (7, 13)}
        DVE_AFTER = {"chain0": (0, 6), "chain1": (1, 7), "masks": (2, 8), "state": (4, 10),
                     "norm2": (5, 11), "apply": (6, 12), "xlo": (7, 13)}
        ACT_AFTER = {"gt": (3, 9), "oT": (4, 10), "fetch": (0, 4), "xhi": (7, 13)}

        PE_BESIDE = {"levels": (4, 99), "o": (5, 99), "wo": (6, 99)}
        DVE_BESIDE = {"masks": (4, 99), "state": (5, 99), "norm2": (6, 99), "apply": (7, 99),
                      "chain0": (3, 6), "chain1": (3, 7), "xlo": (7, 99)}
        ACT_BESIDE = {"gt": (4, 99), "oT": (5, 99), "fetch": (2, 5), "xhi": (7, 99)}
        POOL_BESIDE = {"join": (4, 99), "norm2": (6, 99), "fetch": (2, 5)}
        AHEAD = 4

        def stages(after, u):
            return [(s, k) for s in after for k in range(2) if after[s][k] == u]

        starts = {s.name: 1 for s in (
            xn_ready, stored, abs_done, tile_T, xnT0_ready, xnT1_ready, z_copied, v_stored, o_done,
            state_ready, hid_ready, down_done, hi_ready, lo_ready, tile2_T, xT_ready, gt_ready,
            y_ready, w_T, w_ready)}
        starts[v_done.name] = 2

        def nth(s, n):
            return n + starts.get(s.name, 0)

        def of(c):
            return bass.ds(c, 1)

        def kept(c, a, b):
            return store[:, of(c), a * P:b * P].rearrange("p o n -> p (o n)")

        def tile(c, b):
            return x_sb[:, b, of(c), :].rearrange("p o n -> p (o n)")

        def xT_part(g, k, b, part):
            return xT[:, of(g), part, :, (2 * k + b) * P:(2 * k + b + 1) * P].rearrange("p o t n -> p (o t) n")

        def tiles(ap):
            return ap.rearrange("p (t n) -> p t n", t=DT)

        def in_bank(l):
            return pa[:, l * P:(l + 1) * P] if l < 4 else pb_[:, (l - 4) * P:(l - 3) * P]

        def carry_wait():
            nc.vector.memset(idle[:, :], 0.0)

        block = ctx.enter_context(nc.Block())

        @block.sync
        def _(sp_):
            def load_x(i, par):
                for b in range(B):
                    sp_.dma_start(x_sb[:, b, of(2 * i + par), :],
                                  x_v[:, b, of(2 * i + par), :]).then_inc(x_in[par], 16)

            def load_w(i, par):
                for n in range(3):
                    sp_.dma_start(nat[n][:, bass.ds((2 * i + par) * SL, SL)],
                                  wn_v[n][:, bass.ds((2 * i + par) * SL, SL)]).then_inc(w_in[par], 16)

            load_x(0, 0)
            for s in (xn_ready, v_done, stored, abs_done, tile_T, xnT0_ready, xnT1_ready, z_copied,
                      v_stored, o_done, state_ready, hid_ready, down_done, hi_ready, lo_ready, tile2_T,
                      xT_ready, gt_ready, y_ready, w_T, w_ready):
                sp_.sem_inc(s, starts[s.name])
            load_x(0, 1)
            for dst, w in ((wqk[:, :, 0:K], Wq), (wqk[:, :, K:2 * K], Wk), (wbd[:, :, 0:K], Wb),
                           (wbd[:, :, K:2 * K], Wd), (wv[:, :, :], Wv)):
                sp_.dma_start(dst, w.rearrange("(t p) k -> p t k", p=P)).then_inc(weights_in, 16)
            for b in range(B):
                rows = slice(b * K, (b + 1) * K)
                sp_.dma_start(bias[rows, 0:1], bb.rearrange("(k o) -> k o", o=1)).then_inc(bias_in, 16)
                sp_.dma_start(bias[rows, 1:2], bd.rearrange("(k o) -> k o", o=1)).then_inc(bias_in, 16)
            sp_.dma_start(wo[:, :], Wo).then_inc(wo_in, 16)
            load_w(0, 0)
            load_w(0, 1)
            with sp_.Fori(0, C // 2 - 1) as i:
                for par in range(2):
                    sp_.wait_ge(x_in[par], 32 * (i + 1))
                    load_x(i + 1, par)
                    sp_.wait_ge(w_in[par], 48 * (i + 1))
                    load_w(i + 1, par)

            with sp_.Fori(0, G) as g:
                for m in range(4):
                    sp_.wait_ge(y_ready, nth(y_ready, 4 * g + m + 1))
                    sp_.dma_start(out_v[:, m % 2, of(2 * g + m // 2), :],
                                  x_sb[:, m % 2, of(2 * g + m // 2), :]).then_inc(y_stored, 16)
            sp_.wait_ge(y_stored, 16 * 4 * G)

        @block.gpsimd
        def _(pool):
            st = Steps()

            def link(ins):
                ins.then_inc(pool_steps, 1)
                pool.wait_ge(pool_steps, st.next())

            nc.gpsimd.memset(ones[:, :], 1.0)
            for n, value in enumerate((LN_EPS, -0.5, -0.5, 1.5, -0.5 * XS, 1.5 * XS)):
                nc.gpsimd.memset(rconst[:, n, :], value)
            nc.gpsimd.memset(tmk[:, :], 1.0)
            nc.gpsimd.memset(cur[:, 0:4 * P], 0.0)
            nc.gpsimd.memset(S[:, :], 0.0)
            link(nc.gpsimd.memset(ident[:, :], 0.0))
            link(nc.gpsimd.affine_select(out=ident[:, :], in_=ident[:, :], compare_op=ALU.not_equal,
                                             fill=1.0, base=0, pattern=[[-1, P]], channel_multiplier=1))
            nc.gpsimd.tensor_copy(pos16[:, :], ident[:, :])
            nc.gpsimd.tensor_scalar(neg16[:, :], ident[:, :], -1.0, 0.0, ALU.mult, ALU.add).then_inc(consts, 1)

            def make_masks(levels):
                for l in levels:
                    h, n = 2 ** l, P // 2 ** (l + 1)
                    m = level(mask[:, l, :], l)
                    link(nc.gpsimd.affine_select(out=m, in_=level(ones[:, 0:P // 2], l),
                                                     compare_op=ALU.is_ge, fill=0.0, base=0,
                                                     pattern=[[-2 * h, n], [0, h]], channel_multiplier=1))
                    nc.gpsimd.affine_select(out=m, in_=m, compare_op=ALU.is_gt, fill=0.0, base=h,
                                            pattern=[[2 * h, n], [0, h]], channel_multiplier=-1)

            def rstd(mv, rs, scale, out_sem):
                k = 2 if scale == 1.0 else 4

                def op(out, a, b, alu):
                    return nc.gpsimd.tensor_tensor(out[:, :], a, b, alu)
                link(op(ve, mv[:, :, 1], rconst[:, 0, :], ALU.add))
                link(op(rs0, ve[:, :], rconst[:, 1, :], ALU.pow))
                link(op(rs1, rs0[:, :], rs0[:, :], ALU.mult))
                link(op(rs1, rs1[:, :], ve[:, :], ALU.mult))
                link(op(rs1, rs1[:, :], rconst[:, k, :], ALU.mult))
                link(op(rs1, rs1[:, :], rconst[:, k + 1, :], ALU.add))
                op(rs, rs1[:, :], rs0[:, :], ALU.mult).then_inc(out_sem, 1)
            NORM_STEPS, GATE_STEPS, FETCH_STEPS, JOIN_STEPS = 6, 2, NL - 1, NL - 1

            def norm(c):
                pool.wait_ge(stats_ready, c + 1)
                pool.wait_ge(xn_ready, nth(xn_ready, c))
                rstd(mv, rs, 1.0, rstd_ready)

            def gates(c):
                pool.wait_ge(z_ready, c + 1)
                pool.wait_ge(u_ready, c + 1)
                nc.gpsimd.tensor_tensor(sp[:, 0, :], u_1[:, :], e_d[:, :], ALU.subtract)
                link(nc.gpsimd.tensor_tensor(sp[:, 1, :], z_pos[:, :], z_ln[:, :], ALU.add))
                link(nc.gpsimd.tensor_tensor(sp[:, 1, :], sp[:, 1, :], sp[:, 0, :], ALU.subtract))
                nc.gpsimd.tensor_tensor(kept(c, 2, 3), sp[:, 1, :], zkd[:, 0, :], ALU.mult)
                nc.gpsimd.tensor_copy(kept(c, 0, 1), zqb[:, 0, :])
                pool.wait_ge(beta_ready, c + 1)
                nc.gpsimd.tensor_tensor(kept(c, 1, 2), zqb[:, 0, :], kept(c, 3, 4),
                                        ALU.mult).then_inc(stored, 1)

            def fetch(c):
                pool.wait_ge(state_ready, nth(state_ready, c))
                for l in range(NL):
                    t = (kept(c, 3, 4) if l == 0 else tot_of(l)).rearrange("p (n two) -> p n two", two=2)
                    n = P // 2 ** (l + 1)
                    m = factors(l).rearrange("p (a n two) -> p a n two", a=3, two=2)
                    prod = nc.gpsimd.tensor_tensor(tot_of(l + 1), t[:, :, 0], t[:, :, 1], ALU.mult)
                    if l < NL - 1:
                        prod.then_inc(pool_steps, 1)
                    nc.gpsimd.tensor_copy(m[:, 0:2, :, 1], t[:, :, 0].unsqueeze(1).broadcast_to([P, 2, n]))
                    last = nc.gpsimd.tensor_copy(m[:, 2, :, 0], t[:, :, 1])
                    if l < NL - 1:
                        pool.wait_ge(pool_steps, st.next())
                last.then_inc(factors_ready, 1)

            def join(c):
                pool.wait_ge(masked, c + 1)
                for l in range(NL):
                    a = second(sc[:, DIAG:DIAG + 2 * P], l)
                    last = nc.gpsimd.tensor_tensor(
                        a, a, sc[:, l * P:(l + 1) * P].rearrange("p (b n h) -> p b n h", b=B, h=2 ** l), ALU.add)
                    if l < NL - 1:
                        link(last)
                last.then_inc(scores_ready, 1)

            def norm2(c):
                pool.wait_ge(stats2_ready, c + 1)
                rstd(mv2, rs2, XS, rstd2_ready)

            def attn(s, c):
                {"fetch": fetch, "join": join, "norm2": norm2}[s](c)

            make_masks(range(4, NL))
            norm(0)
            make_masks(range(2, 4))
            norm(1)
            make_masks(range(2))
            for c in range(C):
                if c + 2 < C:
                    norm(c + 2)
                for s, k in stages(POOL_BESIDE, c):
                    attn(s, k)
                gates(c)
            attn("join", 1)
            attn("norm2", 1)

            def group(g):
                fetch(2 * g + 2)
                join(2 * g + 2)
                fetch(2 * g + 3)
                norm2(2 * g + 2)
                join(2 * g + 3)
                norm2(2 * g + 3)

            group(0)
            with pool.Fori(1, G - 1) as g:
                st.loop(g - 1, 2 * (FETCH_STEPS + JOIN_STEPS + NORM_STEPS))
                group(g)
                st.end(G - 2)

        @block.scalar
        def _(act):
            st = Steps()

            def link(ins):
                ins.then_inc(act_steps, 1)
                act.wait_ge(act_steps, st.next())

            nc.scalar.preload_act_table_set("natural_log_exp_and_others")

            def evacuate_T(c):
                par = c % 2
                act.wait_ge(tile_T, nth(tile_T, 2 * c + 1))
                act.wait_ge(v_done, nth(v_done, c - 1))
                nc.scalar.activation(xnT[:, par, :, 0, :], tiles(bank[0][:, :]), ACT.Copy).then_inc(xnT0_ready, 1)

            def exps(c):
                act.wait_ge(stored, nth(stored, c))
                act.wait_ge(proj_done, c + 1)
                z = bank[2][:, :].rearrange("p (a b n) -> p a b n", a=2, b=B)
                for b in range(B):
                    rows = slice(b * K, (b + 1) * K)
                    nc.scalar.activation(zqb[rows, :, :], z[0:K, :, b, :], ACT.Copy)
                    last = nc.scalar.activation(zkd[rows, :, :], z[K:2 * K, :, b, :], ACT.Copy)
                last.then_inc(z_copied, 1)
                act.wait_ge(z_copied, nth(z_copied, c + 1))
                nc.scalar.activation(z_abs[:, :], zkd[:, 1, :], ACT.Abs, bias=bias[:, 1:2])
                nc.scalar.activation(z_pos[:, :], zkd[:, 1, :], ACT.Relu, bias=bias[:, 1:2])
                link(nc.scalar.activation(e_b[:, :], zqb[:, 1, :], ACT.Exp, scale=-1.0,
                                              bias=bias[:, 0:1]))
                link(nc.scalar.activation(e_d[:, :], z_abs[:, :], ACT.Exp, scale=-1.0))
                nc.scalar.activation(z_ln[:, :], e_d[:, :], ACT.Ln, bias=ones[:, 0:1]).then_inc(z_ready, 1)

            def absum(c):
                act.wait_ge(w_in[c % 2], 48 * (c // 2 + 1))
                act.wait_ge(abs_done, nth(abs_done, c))
                for n in range(3):
                    last = nc.scalar.activation(abs_out[n], nat[n][:, bass.ds(c * SL, SL)], ACT.Abs,
                                                accum_out=abs_part[:, n, of(c)])
                last.then_inc(abs_done, 1)

            def prep(j, matrices=range(3)):
                for n in matrices:
                    src = bank[n] if j < AHEAD else pd
                    act.wait_ge(w_T, nth(w_T, 3 * j + n + 1))
                    if n < 2:
                        dst = wT[n][:, :, j * P:(j + 1) * P]
                    else:
                        dst = wT[2][:, j, :].rearrange("p (n t) -> p t n", t=DT)
                    nc.scalar.activation(dst, tiles(src[:, :]), ACT.Copy).then_inc(w_ready, 1)

            def attn(s, g, k):
                c = 2 * g + k
                if s == "fetch":
                    act.wait_ge(v_stored, nth(v_stored, c + 1))
                    act.wait_ge(stored, nth(stored, c + 1))
                    act.wait_ge(o_done, nth(o_done, c))
                    for b in range(B):
                        rows = slice(b * K, (b + 1) * K)
                        nc.scalar.activation(
                            cur[rows, 0:4 * P].rearrange("p (a b n) -> p a b n", a=2, b=B)[:, :, b, :],
                            store[rows, of(c), 0:2 * P].rearrange("p o (a n) -> p (o a) n", a=2), ACT.Copy)
                    nc.scalar.activation(cur[:, 4 * P:8 * P], kept(c, 2, 6), ACT.Copy).then_inc(gbv_ready, 1)
                if s == "gt":
                    act.wait_ge(levels_done, c + 1)
                    nc.scalar.activation(GT[:, :], pe_[:, 0:P], ACT.Copy).then_inc(gt_ready, 1)
                if s == "oT":
                    act.wait_ge(o_done, nth(o_done, c + 1))
                    nc.scalar.activation(oT[:, :, :], pc[:, 0:B * P].rearrange("p (b n) -> p b n", b=B),
                                         ACT.Copy).then_inc(oT_ready, 1)
                if s == "xhi":
                    if isinstance(g, int) and g == 1:
                        act.wait_ge(quantised, 3 * 4 + 2)
                    for b in range(B):
                        act.wait_ge(tile2_T, nth(tile2_T, 2 * c + b + 1))
                        nc.scalar.activation(xT_part(g, k, b, 0), tiles(pab[b][:, :]),
                                             ACT.Copy).then_inc(xhi_ready, 1)

            act.wait_ge(consts, 1)
            evacuate_T(0)
            act.wait_ge(bias_in, 64)
            link(nc.scalar.activation(bias[:, 0:1], bias[:, 0:1], ACT.Copy, scale=-1.0))
            for c in range(C):
                if c + 1 < C:
                    evacuate_T(c + 1)
                for s, k in stages(ACT_BESIDE, c):
                    attn(s, 0, k)
                absum(c)
                exps(c)
            attn("gt", 0, 1)
            prep(0)
            attn("oT", 0, 1)
            prep(1)
            prep(2)
            prep(3)
            attn("xhi", 0, 1)

            def group(g, work, weights=False):
                for u in range(UNITS):
                    if weights and 1 <= u <= HT - AHEAD:
                        prep(u + AHEAD - 1, [2])
                    if u < HT:
                        act.wait_ge(gate_done, g * HT + u + 1)
                        act.wait_ge(hid_ready, nth(hid_ready, g * HT + max(u - 1, 0)))
                        nc.scalar.activation(sig[:, u % 2, :], bank[2 * u % 3][:, :], ACT.Sigmoid,
                                             scale=1.0 / XS).then_inc(sig_ready, 1)
                    if 1 <= u <= HT:
                        act.wait_ge(hid_ready, nth(hid_ready, g * HT + u))
                        if u == 1:
                            act.wait_ge(down_done, nth(down_done, g * DT))
                        nc.scalar.activation(hid[:, 0, u - 1, :], hid32[:, (u - 1) % 2, :],
                                             ACT.Copy).then_inc(hi_ready, 1)
                    if weights and u + AHEAD < HT:
                        prep(u + AHEAD, [0, 1])
                    if work:
                        for s, k in stages(ACT_AFTER, u):
                            attn(s, g + 1, k)

            group(0, True, True)
            with act.Fori(1, G - 1) as g:
                group(g, True)
            group(G - 1, False)

        @block.vector
        def _(dve):
            st = Steps()

            def link(ins):
                ins.then_inc(dve_steps, 1)
                dve.wait_ge(dve_steps, st.next())

            def statistics(c, stats, mv, out_sem):
                carry_wait()
                for b in range(B):
                    last = nc.vector.bn_stats(stats[:, b, :], tile(c, b))
                link(last)
                carry_wait()
                for b in range(B):
                    last = nc.vector.bn_aggr(mv[:, b, :], stats[:, b, :])
                last.then_inc(out_sem, 1)

            def normalise(c, xn, mv, rs, out_sem):
                for b in range(B):
                    last = nc.vector.tensor_scalar(xn[:, b, :], tile(c, b), mv[:, b, 0:1], rs[:, b:b + 1],
                                                   ALU.subtract, ALU.mult)
                last.then_inc(out_sem, 1)

            def mean_var(c):
                dve.wait_ge(x_in[c % 2], 32 * (c // 2 + 1))
                dve.wait_ge(xn_ready, nth(xn_ready, c))
                statistics(c, stats, mv, stats_ready)

            def apply(c):
                dve.wait_ge(rstd_ready, c + 1)
                dve.wait_ge(tile_T, nth(tile_T, 2 * c))
                normalise(c, xn, mv, rs, xn_ready)

            def evacuate_T(c):
                par = c % 2
                dve.wait_ge(tile_T, nth(tile_T, 2 * c + 2))
                dve.wait_ge(v_done, nth(v_done, c - 1))
                nc.vector.tensor_copy(xnT[:, par, :, 1, :], tiles(bank[1][:, :])).then_inc(xnT1_ready, 1)

            def gates(c):
                dve.wait_ge(v_done, nth(v_done, c + 1))
                nc.vector.tensor_copy(kept(c, 4, 6), pd[:, 0:B * V]).then_inc(v_stored, 1)
                dve.wait_ge(z_ready, c + 1)
                nc.vector.tensor_scalar(u_1[:, :], e_d[:, :], 1.0, -1.0, ALU.add, ALU.add).then_inc(u_ready, 1)
                link(nc.vector.tensor_scalar(e_b[:, :], e_b[:, :], 1.0, None, ALU.add))
                nc.vector.reciprocal(kept(c, 3, 4), e_b[:, :]).then_inc(beta_ready, 1)

            def thresholds():
                link(nc.vector.tensor_scalar(thr[:, 0, :], pd[:, 0:3], 0.5 / (H * D), 0.5 * Q_EPS,
                                             ALU.mult, ALU.add))
                link(nc.vector.tensor_scalar(thr[:, 1, :], thr[:, 0, :], -1.0, None, ALU.mult))

            def quantise(j, matrices=range(3)):
                for n in matrices:
                    if n < 2:
                        piece = tiles(nat[n][:, j * D:(j + 1) * D])
                    else:
                        piece = nat[2].rearrange("p (t q r) -> p t q r", t=DT, r=HT)[:, :, :, j]
                    dve.wait_ge(w_T, nth(w_T, max(0, 3 * (j - 1) + n + 1)))
                    nc.vector.tensor_scalar(tiles(above[:, n, :]), piece, thr[:, 0, n:n + 1], None, ALU.is_gt)
                    nc.vector.tensor_scalar(tiles(below[:, n, :]), piece, thr[:, 1, n:n + 1], None,
                                            ALU.is_lt).then_inc(quantised, 1)

            def chain(c, levels):
                for l in levels:
                    n, h = P // 2 ** (l + 1), 2 ** l
                    link(nc.vector.tensor_tensor(
                        FG(l + 1).rearrange("p (n h) -> p n h", h=h), FG(l).rearrange("p (n h) -> p n h", h=h),
                        factors(l).unsqueeze(2).broadcast_to([P, 6 * n, h]), ALU.mult))

            def attn(s, g, k):
                c = 2 * g + k
                if s == "chain0":
                    dve.wait_ge(factors_ready, c + 1)
                    dve.wait_ge(gbv_ready, c + 1)
                    chain(c, range(0, 4))
                if s == "chain1":
                    chain(c, range(4, NL - 1))
                    l = NL - 1
                    nc.vector.tensor_tensor(
                        FG(NL).rearrange("p (n h) -> p n h", h=2 ** l), FG(l).rearrange("p (n h) -> p n h", h=2 ** l),
                        factors(l).unsqueeze(2).broadcast_to([P, 6, 2 ** l]), ALU.mult).then_inc(chain_ready, 1)
                if s == "masks":
                    dve.wait_ge(levels_done, c + 1)
                    dve.wait_ge(o_done, nth(o_done, c))
                    for first_l, last_l, src in ((0, 4, pa), (4, NL, pb_)):
                        n = last_l - first_l
                        nc.vector.tensor_tensor(
                            sc[:, first_l * P:last_l * P].rearrange("p (l b m) -> p l b m", l=n, b=B),
                            src[:, 0:n * P].rearrange("p (l b m) -> p l b m", l=n, b=B),
                            mask[:, first_l:last_l, :].unsqueeze(2).broadcast_to([P, n, B, P // 2]), ALU.mult)
                    nc.vector.tensor_tensor(
                        sc[:, DIAG:DIAG + 2 * P].rearrange("p (b m) -> p b m", b=B),
                        pc[:, 0:2 * P].rearrange("p (b m) -> p b m", b=B),
                        ident[:, :].unsqueeze(1).broadcast_to([P, B, P]), ALU.mult).then_inc(masked, 1)
                if s == "state":
                    dve.wait_ge(o_done, nth(o_done, c + 1))
                    for b in range(B):
                        rows = slice(b * K, (b + 1) * K)
                        last = nc.vector.scalar_tensor_tensor(
                            S[rows, :], S[rows, :], tot_of(NL)[rows, :], pe_[rows, b * P:(b + 1) * P],
                            ALU.mult, ALU.add)
                    last.then_inc(state_ready, 1)
                if s == "norm2":
                    dve.wait_ge(attn_done, c + 1)
                    for b in range(B):
                        last = nc.vector.tensor_tensor(tile(c, b), tile(c, b), pab[b][:, :], ALU.add)
                    last.then_inc(resid_ready, 1)
                    dve.wait_ge(resid_ready, c + 1)
                    statistics(c, stats2, mv2, stats2_ready)
                if s == "apply":
                    dve.wait_ge(rstd2_ready, c + 1)
                    dve.wait_ge(tile2_T, nth(tile2_T, 2 * c))
                    normalise(c, xn2, mv2, rs2, xn2_ready)
                if s == "xlo":
                    for b in range(B):
                        dve.wait_ge(xhi_ready, 2 * c + b + 1)
                        nc.vector.tensor_tensor(xT_part(g, k, b, 1), tiles(pab[b][:, :]),
                                                xT_part(g, k, b, 0), ALU.subtract).then_inc(xT_ready, 1)
            GATE_STEPS, NORM_STEPS, CHAIN_STEPS = 1, 1, NL - 1

            mean_var(0)
            apply(0)
            mean_var(1)
            evacuate_T(0)
            apply(1)
            for c in range(C):
                if c + 1 < C:
                    evacuate_T(c + 1)
                if c + 2 < C:
                    mean_var(c + 2)
                for s, k in stages(DVE_BESIDE, c):
                    attn(s, 0, k)
                if c + 2 < C:
                    apply(c + 2)
                if c == C - 1:
                    dve.wait_ge(abs_done, nth(abs_done, C))
                    nc.vector.tensor_reduce(abs_sum[:, :], abs_part[:, :, :], AX.X,
                                            ALU.add).then_inc(abs_summed, 1)
                gates(c)
            attn("masks", 0, 1)
            dve.wait_ge(sums_spread, 1)
            thresholds()
            quantise(0)
            quantise(1)
            attn("state", 0, 1)
            quantise(2)
            attn("norm2", 0, 1)
            quantise(3)
            attn("apply", 0, 1)
            attn("xlo", 0, 1)
            quantise(AHEAD, [0, 1])

            def group(g, work, weights=False):
                for u in range(UNITS):
                    if u < HT:
                        dve.wait_ge(up_done, g * HT + u + 1)
                        dve.wait_ge(sig_ready, g * HT + u + 1)
                        dve.wait_ge(hi_ready, nth(hi_ready, g * HT + max(u - 1, 0)))
                        dve.wait_ge(lo_ready, nth(lo_ready, g * HT + max(u - 1, 0)))
                        nc.vector.scalar_tensor_tensor(hid32[:, u % 2, :], bank[(2 * u + 1) % 3][:, :],
                                                       HS / XS, sig[:, u % 2, :], ALU.mult,
                                                       ALU.mult).then_inc(hid_ready, 1)
                    if 1 <= u <= HT:
                        dve.wait_ge(hi_ready, nth(hi_ready, g * HT + u))
                        nc.vector.tensor_tensor(hid[:, 1, u - 1, :], hid32[:, (u - 1) % 2, :],
                                                hid[:, 0, u - 1, :], ALU.subtract).then_inc(lo_ready, 1)
                    if u >= HT:
                        m = u - HT
                        dve.wait_ge(down_done, nth(down_done, g * DT + m + 1))
                        y = tile(2 * g + m // 2, m % 2)
                        nc.vector.scalar_tensor_tensor(y, bank[(2 * HT + m) % 3][:, :], 1.0 / HS, y, ALU.mult,
                                                       ALU.add).then_inc(y_ready, 1)
                    if weights and u + AHEAD < HT:
                        quantise(u + AHEAD, [2])
                    if weights and u + AHEAD + 1 < HT:
                        quantise(u + AHEAD + 1, [0, 1])
                    if work:
                        for s, k in stages(DVE_AFTER, u):
                            attn(s, g + 1, k)

            group(0, True, True)
            with dve.Fori(1, G - 1) as g:
                st.loop(g - 1, 2 * (CHAIN_STEPS + NORM_STEPS))
                group(g, True)
                st.end(G - 2)
            group(G - 1, False)

        @block.tensor
        def _(pe):
            pe.wait_ge(consts, 1)

            def transposes(c):
                pe.wait_ge(xn_ready, nth(xn_ready, c + 1))
                pe.wait_ge(xnT0_ready, nth(xnT0_ready, c))
                pe.wait_ge(xnT1_ready, nth(xnT1_ready, c))
                for b in range(B):
                    for t in range(DT):
                        last = nc.tensor.transpose(bank[b][:, t * P:(t + 1) * P], xn[:, b, t * P:(t + 1) * P],
                                                   ident[:, :])
                    last.then_inc(tile_T, 1)

            def project(c, between=None):
                par = c % 2
                pe.wait_ge(xnT0_ready, nth(xnT0_ready, c + 1))
                pe.wait_ge(xnT1_ready, nth(xnT1_ready, c + 1))
                pe.wait_ge(z_copied, nth(z_copied, c))
                for a, w in enumerate((wqk, wbd)):
                    for t in range(DT):
                        last = nc.tensor.matmul(bank[2][:, a * 256:(a + 1) * 256], w[:, t, :], xnT[:, par, t, :, :],
                                                start=t == 0, stop=t == DT - 1)
                last.then_inc(proj_done, 1)
                if between is not None:
                    attn(between, 0, 0)
                pe.wait_ge(v_stored, nth(v_stored, c))
                for b in range(B):
                    for t in range(DT):
                        last = nc.tensor.matmul(pd[:, b * V:(b + 1) * V], xnT[:, par, t, b, :], wv[:, t, :],
                                                start=t == 0, stop=t == DT - 1)
                last.then_inc(v_done, 1)

            def spread():
                pe.wait_ge(abs_summed, 1)
                pe.wait_ge(v_stored, nth(v_stored, C))
                nc.tensor.matmul(pd[:, 0:3], ones[:, :], abs_sum[:, :], start=True, stop=True
                                 ).then_inc(sums_spread, 1)

            def prep(j, n):
                pe.wait_ge(quantised, 3 * j + n + 1)
                dst = bank[n] if j < AHEAD else pd
                if j < AHEAD:
                    if j == 0 and n == 2:
                        pe.wait_ge(z_copied, nth(z_copied, C))
                    if j > 0:
                        pe.wait_ge(w_ready, nth(w_ready, 3 * (j - 1) + n + 1))
                else:
                    pe.wait_ge(w_ready, nth(w_ready, 3 * j + n))
                for t in range(DT):
                    at = slice(t * P, (t + 1) * P)
                    nc.tensor.matmul(dst[:, at], above[:, n, at], pos16[:, :], start=True, stop=False)
                    last = nc.tensor.matmul(dst[:, at], below[:, n, at], neg16[:, :], start=False, stop=True)
                last.then_inc(w_T, 1)

            def attn(s, g, k):
                c = 2 * g + k
                if s == "levels":
                    pe.wait_ge(chain_ready, c + 1)
                    pe.wait_ge(xT_ready, nth(xT_ready, 2 * c))
                    for l in range(NL):
                        nc.tensor.matmul(in_bank(l), Gk(l), second(F(l), l), start=True, stop=True)
                    nc.tensor.matmul(pc[:, 0:2 * P], Gk(0), cur[:, 0:2 * P], start=True, stop=True)
                    nc.tensor.transpose(pe_[:, 0:P], Gk(NL), ident[:, :]).then_inc(levels_done, 1)
                if s == "o":
                    pe.wait_ge(scores_ready, c + 1)
                    pe.wait_ge(gt_ready, nth(gt_ready, c + 1))
                    pe.wait_ge(state_ready, nth(state_ready, c))
                    nc.tensor.matmul(pc[:, 0:2 * P], S[:, :], F(NL), start=True, stop=False)
                    for b in range(B):
                        nc.tensor.matmul(pc[:, b * P:(b + 1) * P], cur[:, (6 + b) * P:(7 + b) * P],
                                         sc[:, DIAG + b * P:DIAG + (b + 1) * P], start=False, stop=b == B - 1)
                    nc.tensor.matmul(pe_[:, 0:2 * P], GT[:, :], cur[:, 6 * P:8 * P], start=True, stop=True
                                     ).then_inc(o_done, 1)
                if s == "wo":
                    pe.wait_ge(oT_ready, c + 1)
                    for b in range(B):
                        last = nc.tensor.matmul(pab[b][:, :], oT[:, b, :], wo[:, :], start=True, stop=True)
                    last.then_inc(attn_done, 1)
                if s == "t2":
                    pe.wait_ge(xn2_ready, c + 1)
                    for b in range(B):
                        for t in range(DT):
                            last = nc.tensor.transpose(pab[b][:, t * P:(t + 1) * P],
                                                       xn2[:, b, t * P:(t + 1) * P], ident[:, :])
                        last.then_inc(tile2_T, 1)

            transposes(0)
            pe.wait_ge(weights_in, 16 * 5)
            transposes(1)
            project(0)
            pe.wait_ge(wo_in, 16)
            for c in range(1, C):
                if c + 1 < C:
                    transposes(c + 1)
                for s, k in stages(PE_BESIDE, c):
                    attn(s, 0, k)
                project(c, "t2" if c == C - 1 else None)
            spread()
            attn("levels", 0, 1)
            for n in range(3):
                prep(0, n)
            attn("o", 0, 1)
            for n in range(3):
                prep(1, n)
            attn("wo", 0, 1)
            for j in range(2, AHEAD):
                for n in range(3):
                    prep(j, n)
            attn("t2", 0, 1)

            def bank_free(g, n):
                m = n - 3
                if m < 0:
                    if n < 2 and not (isinstance(g, int) and g == 0):
                        pe.wait_ge(y_ready, nth(y_ready, g * DT - 1 + n))
                    return
                if m < 2 * HT:
                    used = hid_ready if m % 2 else sig_ready
                    pe.wait_ge(used, nth(used, g * HT + m // 2 + 1))
                else:
                    pe.wait_ge(y_ready, nth(y_ready, g * DT + m - 2 * HT + 1))

            def group(g, work, weights=False):
                if weights:
                    pe.wait_ge(w_ready, nth(w_ready, 3 * AHEAD))
                pe.wait_ge(xT_ready, nth(xT_ready, 4 * g + 4))
                for u in range(UNITS):
                    if u < HT:
                        pe.wait_ge(w_ready, nth(w_ready, min(3 * (u + 1), 3 * HT) if weights else 3 * HT))
                        for a in range(2):
                            n = 2 * u + a
                            bank_free(g, n)
                            for t in range(DT):
                                for part in range(2):
                                    last = nc.tensor.matmul(
                                        bank[n % 3][:, :], wT[a][:, t, u * P:(u + 1) * P],
                                        xT[:, of(g), part, t, :].rearrange("p o n -> p (o n)"),
                                        start=t == 0 and part == 0, stop=t == DT - 1 and part == 1)
                                if weights and 1 <= u <= HT - AHEAD and (a, t) == (0, 1):
                                    prep(u + AHEAD - 1, 2)
                                if weights and u + AHEAD < HT and (a, t) in ((1, 0), (1, 2)):
                                    prep(u + AHEAD, t // 2)
                            last.then_inc((gate_done, up_done)[a], 1)
                    else:
                        m = u - HT
                        bank_free(g, 2 * HT + m)
                        for part in range(2):
                            for j in range(HT):
                                if m == 0:
                                    part_ready = (hi_ready, lo_ready)[part]
                                    pe.wait_ge(part_ready, nth(part_ready, g * HT + j + 1))
                                last = nc.tensor.matmul(bank[(2 * HT + m) % 3][:, :],
                                                        hid[:, part, j, m * P:(m + 1) * P], wT[2][:, j, :],
                                                        start=part == 0 and j == 0,
                                                        stop=part == 1 and j == HT - 1)
                        last.then_inc(down_done, 1)
                    if work:
                        for s, k in stages(PE_AFTER, u):
                            attn(s, g + 1, k)

            group(0, True, True)
            with pe.Fori(1, G - 1) as g:
                group(g, True)
            group(G - 1, False)


_INS = ['L0_attn_x', 'L0_attn_Wq', 'L0_attn_Wk', 'L0_attn_Wv', 'L0_attn_Wo', 'L0_attn_Wb', 'L0_attn_bb',
        'L0_attn_Wd', 'L0_attn_bd', 'L0_ffn_w1', 'L0_ffn_w2', 'L0_ffn_w3']


def kernel(**inputs):
    import numpy as _np
    import concourse.bacc as _bacc
    from concourse import mybir as _mybir
    from concourse.bass_utils import run_bass_kernel_spmd as _run

    nc = _bacc.Bacc("TRN2", target_bir_lowering=False, num_devices=1,
                    dynamic_dma_scratch_size=1024)
    arrays, args = {}, []
    for name in _INS:
        a = _np.ascontiguousarray(inputs[name])
        arrays[f"in_{name}_dram"] = a
        args.append(nc.dram_tensor(f"in_{name}_dram", a.shape, _mybir.dt.from_np(a.dtype),
                                   kind="ExternalInput").ap())
    x = inputs['L0_attn_x']
    out = nc.dram_tensor("out_0_dram", x.shape, _mybir.dt.float32, kind="ExternalOutput").ap()
    build_gated_delta_ternary_ffn(nc, *args, out)
    r = _run(nc, [arrays], core_ids=[0])
    return r.results[0]["out_0_dram"]
```
